# Optimizing a Trainium2 kernel written in Bass

```python
import numpy as np
import jax
import jax.numpy as jnp

def _softmax(x, axis=-1):
    return jax.nn.softmax(x, axis=axis)

def _gelu(x):
    return jax.nn.gelu(x, approximate=True)

def _silu(x):
    return jax.nn.silu(x)

def _sigmoid(x):
    return jax.nn.sigmoid(x)

def _layernorm(x, axis=-1, eps=1e-05):
    m = jnp.mean(x, axis=axis, keepdims=True)
    v = jnp.var(x, axis=axis, keepdims=True)
    return (x - m) / jnp.sqrt(v + eps)

def _scatter_add(tgt, idx, src, axis=0):
    return tgt.at[idx].add(src)

def _segment_sum(src, seg, n):
    return jax.ops.segment_sum(src, seg, n)
kernel_name = 'mk_flamingo_gated_d1_seqx_r4_5069a5'

def setup_inputs(seed: int=0):
    np.random.seed(seed)
    _w = jnp.asarray

    def _rec_inputs():
        import jax
        import jax.numpy as jnp
        _rk = jax.random.key(seed)
        x = 7.22e-05 + 1 * jax.random.normal(jax.random.fold_in(_rk, 1), (8, 512, 256), jnp.float32)
        _lenS = 512 - jax.random.randint(jax.random.fold_in(_rk, 7), (8,), 0, max(1, 512 // 4) + 1, jnp.int32)
        _lenS2 = 512 - jax.random.randint(jax.random.fold_in(_rk, 8), (8,), 0, max(1, 512 // 4) + 1, jnp.int32)
        _ctx_1024P = jax.random.normal(jax.random.fold_in(_rk, 11), (8, 16, 256), jnp.float32)
        _ctx_1024c = jax.random.dirichlet(jax.random.fold_in(_rk, 511), 0.3 * jnp.ones((16,), jnp.float32), (8, 512))
        _ctx_1024t = jnp.einsum('bsk,bkd->bsd', _ctx_1024c, _ctx_1024P)
        _ctx_1024t = _ctx_1024t * jax.lax.rsqrt(jnp.mean(jnp.square(_ctx_1024t)) + 1e-12) * 0.953939
        ctx_1024 = 4.13588e-05 + 0.999923 * (_ctx_1024t + 0.3 * jax.random.normal(jax.random.fold_in(_rk, 611), (8, 512, 256), jnp.float32))
        _g = jax.random.normal(jax.random.fold_in(_rk, 9001), (2, 1), jnp.float32)
        _g = jnp.sign(_g) * jnp.maximum(jnp.abs(_g), 1.0) + (_g == 0) * 1.0
        g_xattn = _g[0]
        g_ffn = _g[1]
        return (x, ctx_1024, g_xattn, g_ffn)
    x, ctx_1024, g_xattn, g_ffn = _rec_inputs()

    def _L0_xattn_setup():
        import jax, jax.numpy as jnp
        import numpy as np
        N_HEAD = 16
        key = jax.random.key(seed)
        ks = jax.random.split(key, 5)
        b, l, d = (4, 512, 256)
        dh = d // N_HEAD
        return {'q': jax.random.normal(ks[0], (b, l, d), dtype=jnp.float32), 'kv': jax.random.normal(ks[1], (b, l, d), dtype=jnp.float32), 'Wq': jax.random.normal(ks[2], (d, d), dtype=jnp.float32) * 0.02, 'Wkv': jax.random.normal(ks[3], (2 * dh, d), dtype=jnp.float32) * 0.02, 'Wc': jax.random.normal(ks[4], (d, d), dtype=jnp.float32) * 0.02}
    _L0_xattn_all = _L0_xattn_setup()
    _L0_xattn_in = {k: v for k, v in _L0_xattn_all.items() if k in ('Wq', 'Wkv', 'Wc')}
    del _L0_xattn_all

    def _L0_ffn_setup():
        import jax, jax.numpy as jnp
        import numpy as np
        D_MODEL = 256
        M = 4
        NUM_EXPERTS = 8
        TOP_K = 2
        B, T = (2, 512)
        key = jax.random.key(seed)
        ks = jax.random.split(key, 4)
        d_ff = D_MODEL * M
        x = jax.random.normal(ks[0], (B, T, D_MODEL), dtype=jnp.float32)
        gate_w = jax.random.normal(ks[1], (D_MODEL, NUM_EXPERTS), dtype=jnp.float32) * 0.02
        w1 = jax.random.normal(ks[2], (NUM_EXPERTS, D_MODEL, d_ff), dtype=jnp.float32) * 0.02
        b1 = jnp.zeros((NUM_EXPERTS, d_ff), dtype=jnp.float32)
        w2 = jax.random.normal(ks[3], (NUM_EXPERTS, d_ff, D_MODEL), dtype=jnp.float32) * 0.02
        b2 = jnp.zeros((NUM_EXPERTS, D_MODEL), dtype=jnp.float32)
        return {'x': x, 'gate_w': gate_w, 'w1': w1, 'b1': b1, 'w2': w2, 'b2': b2}
    _L0_ffn_all = _L0_ffn_setup()
    _L0_ffn_in = {k: v for k, v in _L0_ffn_all.items() if k in ('gate_w', 'w1', 'b1', 'w2', 'b2')}
    del _L0_ffn_all
    return {'x': x, 'ctx_1024': ctx_1024, 'g_xattn': g_xattn, 'g_ffn': g_ffn, 'L0_xattn_Wq': _L0_xattn_in['Wq'], 'L0_xattn_Wkv': _L0_xattn_in['Wkv'], 'L0_xattn_Wc': _L0_xattn_in['Wc'], 'L0_ffn_gate_w': _L0_ffn_in['gate_w'], 'L0_ffn_w1': _L0_ffn_in['w1'], 'L0_ffn_b1': _L0_ffn_in['b1'], 'L0_ffn_w2': _L0_ffn_in['w2'], 'L0_ffn_b2': _L0_ffn_in['b2']}

def reference(x, ctx_1024, g_xattn, g_ffn, L0_xattn_Wq, L0_xattn_Wkv, L0_xattn_Wc, L0_ffn_gate_w, L0_ffn_w1, L0_ffn_b1, L0_ffn_w2, L0_ffn_b2):
    import jax
    import jax.numpy as jnp

    def _L0_xattn_ref(q, kv, Wq, Wkv, Wc):
        import jax, jax.numpy as jnp
        import numpy as np
        N_HEAD = 16
        b, l, d = q.shape
        h = N_HEAD
        dh = d // h
        qp = jnp.einsum('bld,ed->ble', q, Wq)
        scores = jnp.einsum('bld,bmd->blm', qp, kv)
        idx = jnp.argmax(scores, axis=-1)
        mem = jnp.take_along_axis(kv, idx[..., None], axis=1)
        mkv = jnp.einsum('bld,ed->ble', mem, Wkv)
        mk, mv = jnp.split(mkv, 2, axis=-1)
        qh = qp.reshape(b, l, h, dh).transpose(0, 2, 1, 3)
        scale = 1.0 / np.sqrt(dh).astype(np.float32)
        logits = jnp.einsum('bhld,bmd->bhlm', qh, mk) * scale
        attn = jax.nn.softmax(logits, axis=-1)
        out = jnp.einsum('bhlm,bmd->bhld', attn, mv)
        out = out.transpose(0, 2, 1, 3).reshape(b, l, d)
        return jnp.einsum('bld,ed->ble', out, Wc)

    def _L0_ffn_ref(x, gate_w, w1, b1, w2, b2):
        import jax, jax.numpy as jnp
        import numpy as np
        D_MODEL = 256
        M = 4
        NUM_EXPERTS = 8
        TOP_K = 2
        B, T = (2, 512)
        Bb, Tt, D = x.shape
        E = w1.shape[0]
        N = Bb * Tt
        logits = jnp.einsum('btd,de->bte', x, gate_w)
        top_v, top_i = jax.lax.top_k(logits, TOP_K)
        top_w = jax.nn.softmax(top_v, axis=-1)
        xf = x.reshape(N, D)
        idx = top_i.reshape(N, TOP_K)
        wts = top_w.reshape(N, TOP_K)
        comb = jnp.zeros((N, E), dtype=x.dtype).at[jnp.arange(N)[:, None], idx].add(wts)
        out = jnp.zeros((N, D), dtype=x.dtype)
        for e in range(E):
            h = jax.nn.gelu(xf @ w1[e] + b1[e], approximate=False)
            out = out + comb[:, e:e + 1] * (h @ w2[e] + b2[e])
        return out.reshape(Bb, Tt, D)
    x = x + jnp.tanh(g_xattn[0]) * _L0_xattn_ref(_layernorm(x, axis=-1), ctx_1024, L0_xattn_Wq, L0_xattn_Wkv, L0_xattn_Wc)
    x = x + jnp.tanh(g_ffn[0]) * _L0_ffn_ref(_layernorm(x, axis=-1), L0_ffn_gate_w, L0_ffn_w1, L0_ffn_b1, L0_ffn_w2, L0_ffn_b2)
    return x

_drawn_inputs = setup_inputs


def setup_inputs(seed=0):
    import zlib

    import numpy as np

    out = dict(_drawn_inputs(seed))
    spreads = {'L0_ffn_b1': (0.0, 0.323), 'L0_ffn_b2': (0.0, 0.1)}
    factors = {'L0_xattn_Wq': 6.068}
    for name, (base, spread) in spreads.items():
        noise = np.random.default_rng([zlib.crc32(name.encode()), seed]).standard_normal(out[name].shape)
        drawn = base * np.exp(spread * noise) if base else spread * noise
        out[name] = jnp.asarray(drawn.astype(out[name].dtype))
    for name, factor in factors.items():
        out[name] = (out[name] * factor).astype(out[name].dtype)
    return out
```

```python
from contextlib import ExitStack

import concourse.bass as bass
from concourse import mybir

P = 128
B, L, D = 8, 512, 256
H = 16
DH = D // H
E, F = 8, 1024
LT, KT, FC = L // P, D // P, F // P
V1 = DH + 1
EPS = 1e-5
SCALE = DH ** -0.5

ROW_PAD = 3 * DH
ROW_MAX = 96
STACK = ROW_MAX + 2
FAR = 1e30

TILE = 2 * P
N_TILES = (2 * B * L + E * (TILE - 1)) // TILE
QUEUE = B * L + TILE
DUMMY = E * QUEUE
ROW = D + 4
NO_TOKEN = 65536.0

F32, BF16, I32, U32 = (mybir.dt.float32, mybir.dt.bfloat16, mybir.dt.int32, mybir.dt.uint32)
F16 = mybir.dt.float16
ALU = mybir.AluOpType
ACT = mybir.ActivationFunctionType
AX = mybir.AxisListType


class Chain:

    def __init__(self, engine, sem):
        self.engine, self.sem, self.n = engine, sem, 0

    def step(self, instruction):
        instruction.then_inc(self.sem, 1)
        self.n += 1

    def settle(self):
        self.engine.wait_ge(self.sem, self.n)

    def then(self, instruction):
        self.step(instruction)
        self.settle()

    def restart(self):
        self.settle()
        self.engine.sem_clear(self.sem)
        self.n = 0


class Shared:
    pass


class AttendSemaphores:

    def __init__(self, sem, nt):
        def of(name):
            return sem(f"{name}_{nt}")

        self.stack_ones = of("stack_ones")
        self.logits_b_ready = of("logits_b_ready")
        self.max_taken = of("max_taken")
        self.max_ready = of("max_ready")
        self.max_turned = of("max_turned")
        self.max_copied = of("max_copied")
        self.max_stored = of("max_stored")
        self.logits_ready = of("logits_ready")
        self.exp_ready = of("exp_ready")
        self.prob_hi_ready = of("prob_hi_ready")
        self.prob_lo_dve = of("prob_lo_dve")
        self.prob_lo_pool = of("prob_lo_pool")
        self.pv_done = of("pv_done")
        self.heads_ready = of("heads_ready")
        self.heads_turned = of("heads_turned")
        self.heads_t_ready = of("heads_t_ready")
        self.y_ready = of("y_ready")
        self.x1_ready = of("x1_ready")
        self.x1_stored = of("x1_stored")
        self.moments_ready = of("moments_ready")
        self.std2_ready = of("std2_ready")
        self.rows_ready = of("rows_ready")
        self.rows_turned = of("rows_turned")
        self.rows_t_ready = of("rows_t_ready")
        self.gate_ready = of("gate_ready")
        self.gap_ready = of("gap_ready")
        self.ratio_ready = of("ratio_ready")
        self.either_ready = of("either_ready")
        self.ranked = of("ranked")
        self.slots_ready = of("slots_ready")
        self.scattered = of("scattered")
        self.attend_steps = of("attend_steps")
        self.attend_pool_steps = of("attend_pool_steps")
        self.x_again = of("x_again")
        self.constants2 = of("constants2")


def program(nc, x, ctx_t, g, wq_t, wkv_t, wc_t, gate_w, w1, b1_t, w2, b2, out):
    k = Shared()
    k.ctx_t, k.g, k.wq_t, k.wkv_t, k.wc_t, k.gate_w = ctx_t, g, wq_t, wkv_t, wc_t, gate_w
    k.w1, k.b1_t, k.w2, k.b2, k.out = w1, b1_t, w2, b2, out
    k.q_split = nc.dram_tensor("q_split", (B, 2, D, L), BF16, kind="Internal").ap()
    k.keys = nc.dram_tensor("keys", (B, STACK, L), BF16, kind="Internal").ap()
    k.values = nc.dram_tensor("values", (B, P, LT * 2 * V1), BF16, kind="Internal").ap()
    k.queue = nc.dram_tensor("queue", (DUMMY + TILE, ROW), F32, kind="Internal").ap()
    k.out_rows = out.rearrange("b l d -> (b l) d")
    k.x_tiles = x.rearrange("b (t p) d -> b p t d", p=P)

    with ExitStack() as whole:
        def sem(name):
            return whole.enter_context(nc.semaphore(name))

        def sb(stack, name, shape, dtype=F32):
            return stack.enter_context(nc.sbuf_tensor(name, shape, dtype))

        def ps(stack, name, shape, dtype=F32):
            return stack.enter_context(nc.psum_tensor(name, shape, dtype))

        k.w1_split = sb(whole, "w1_split", [P, E, 2, KT, F], BF16)
        k.w2_split = sb(whole, "w2_split", [P, E, 2, FC, D], BF16)
        k.n_chosen = sb(whole, "n_chosen", [P, B])
        k.wide = sb(whole, "wide", [1, 1], I32)
        k.ident = sb(whole, "ident", [P, P])
        k.ident_bf = sb(whole, "ident_bf", [P, P], BF16)
        k.before = sb(whole, "before", [P, P], BF16)
        k.ones_bf = sb(whole, "ones_bf", [P, P], BF16)
        k.ones_f = sb(whole, "ones_f", [P, LT + 1])
        k.tanh_g = sb(whole, "tanh_g", [P, 2])
        k.wc_sb = sb(whole, "wc_sb", [P, KT, D])
        k.gate_sb = sb(whole, "gate_sb", [P, KT, E])
        k.expert_no = sb(whole, "expert_no", [P, E])
        k.queue_at = sb(whole, "queue_at", [P, E])
        k.n_queued = sb(whole, "n_queued", [P, E])

        k.consts_loaded = sem("consts_loaded")

        select(nc, k, sem, sb, ps)
        attend(nc, k, sem, sb, ps)
        experts(nc, k, sem, sb, ps)


def select(nc, k, sem, sb, ps):
    with ExitStack() as own:
        wq_sb = sb(own, "wq_sb", [P, KT, D])
        wkv_sb = sb(own, "wkv_sb", [P, KT, 2 * DH])
        column = sb(own, "column", [P, L], F16)
        eps = sb(own, "eps", [P, 1])
        key_mul, key_add = sb(own, "key_mul", [STACK, 1]), sb(own, "key_add", [STACK, 1])
        w_stage = [sb(own, f"w_stage{s}", [P, 1024]) for s in range(2)]
        x_sb = [sb(own, f"x_sb{s}", [P, LT, D]) for s in range(2)]
        xn = sb(own, "xn", [P, LT, D])
        xn_t = sb(own, "xn_t", [P, KT, L])
        ctx_sb = [sb(own, f"ctx_sb{s}", [P, KT, L]) for s in range(2)]
        q_t = [sb(own, f"q_t{s}", [P, KT, L]) for s in range(2)]
        q_hl = sb(own, "q_hl", [P, KT, 2, L], BF16)
        chosen = sb(own, "chosen", [P, LT, L], BF16)
        place = sb(own, "place", [P, LT, L], BF16)
        stats, moments = sb(own, "stats", [P, LT, 6]), sb(own, "moments", [P, LT, 2])
        rstd = sb(own, "rstd", [P, LT])
        top8, top8_at = sb(own, "top8", [P, LT, 8]), sb(own, "top8_at", [P, LT, 8], U32)
        best = sb(own, "best", [P, LT])
        kv = sb(own, "kv", [P, LT, 2 * DH])
        key_cols = sb(own, "key_cols", [P, LT, STACK], BF16)
        value_f = sb(own, "value_f", [P, LT, V1])
        value_cols = sb(own, "value_cols", [P, LT, 2 * V1], BF16)
        key_out = sb(own, "key_out", [STACK, L], BF16)
        value_out = sb(own, "value_out", [P, LT * 2 * V1], BF16)
        count, used = sb(own, "count", [P, LT]), sb(own, "used", [P, LT], BF16)
        unused = sb(own, "unused", [P, LT])
        total, offset = sb(own, "total", [P, LT]), sb(own, "offset", [P, LT + 1])
        position = sb(own, "position", [P, LT])
        most = sb(own, "most", [P, 1])

        ps_t = ps(own, "ps_t", [P, KT, L])
        ps_q = ps(own, "ps_q", [P, KT, L])
        ps_s = [ps(own, f"ps_s{s}", [P, L]) for s in range(2)]
        ps_k = ps(own, "ps_k", [P, L])
        ps_m = ps(own, "ps_m", [P, L])
        ps_kv = ps_m[:, 0:LT * 2 * DH].rearrange("p (t c) -> p t c", t=LT)
        ps_count = ps_m[:, 128:128 + LT]
        ps_rank, ps_total = ps_m[:, 132:132 + LT], ps_m[:, 136:136 + LT]
        ps_v = ps_m[:, 144:144 + LT * 2 * V1].rearrange("p (t c) -> p t c", t=LT)

        x_loaded = [sem(f"x_loaded{s}") for s in range(2)]
        ctx_loaded = [sem(f"ctx_loaded{s}") for s in range(2)]
        w_loaded = [sem(f"w_loaded{s}") for s in range(2)]
        w_hi = sem("w_hi")
        steps, pool_steps = sem("select_steps"), sem("select_pool_steps")
        pool_ready, tanh_ready = sem("pool_ready"), sem("tanh_ready")
        stats_ready, std_ready, xn_ready = sem("stats_ready"), sem("std_ready"), sem("xn_ready")
        xn_turned, xn_t_ready = sem("xn_turned"), sem("xn_t_ready")
        q_ready, q_copied, q_hi, q_lo = sem("q_ready"), sem("q_copied"), sem("q_hi"), sem("q_lo")
        q_stored = sem("q_stored")
        kv_ready, scores_ready, scores_read = sem("kv_ready"), sem("scores_ready"), sem("scores_read")
        chosen_ready, counts_ready, used_ready = sem("chosen_ready"), sem("counts_ready"), sem("used_ready")
        ranks_ready, place_ready, packed = sem("ranks_ready"), sem("place_ready"), sem("packed")
        kv_copied, kv_stored = sem("kv_copied"), sem("kv_stored")

        block = own.enter_context(nc.Block())

        def over_batches(engine, ahead, body):
            ahead(0, 0)
            body(0, 0, True)
            body(1, 1, True)
            with engine.Fori(1, B // 2 - 1) as j:
                for s in range(2):
                    body(2 * j + s, s, True)
            body(B - 2, 0, True)
            body(B - 1, 1, False)

        def w_piece(i, c):
            e = bass.ds(i, 1)
            if c < 2:
                hi, lo = (k.w1_split[:, e, n, c, :].rearrange("p a f -> p (a f)") for n in range(2))
                return hi, lo, w_stage[c % 2][:]
            t = slice((c - 2) * FC // 2, (c - 1) * FC // 2)
            hi, lo = (k.w2_split[:, e, n, t, :].rearrange("p a t d -> p (a t) d") for n in range(2))
            return hi, lo, w_stage[c % 2][:].rearrange("p (t d) -> p t d", d=D)

        w1_flat, w2_flat = k.w1.rearrange("e d f -> (e d f)"), k.w2.rearrange("e f d -> (e f d)")

        @block.sync
        def _(sp):
            sp.dma_start(x_sb[0][:], k.x_tiles[0]).then_inc(x_loaded[0], 16)
            sp.dma_start(wq_sb[:], k.wq_t.rearrange("(t p) n -> p t n", p=P)).then_inc(k.consts_loaded, 16)
            sp.dma_start(wkv_sb[:], k.wkv_t.rearrange("(t p) n -> p t n", p=P)).then_inc(k.consts_loaded, 16)
            sp.dma_start(k.tanh_g[:], k.g[0:1, :].to_broadcast([P, 2])).then_inc(k.consts_loaded, 16)
            sp.dma_start(ctx_sb[0][:], k.ctx_t[0].rearrange("(t p) n -> p t n", p=P)).then_inc(ctx_loaded[0], 16)
            sp.dma_start(k.wc_sb[:], k.wc_t.rearrange("(t p) n -> p t n", p=P)).then_inc(k.consts_loaded, 16)
            sp.dma_start(k.gate_sb[:], k.gate_w.rearrange("(t p) n -> p t n", p=P)).then_inc(k.consts_loaded, 16)

            def load_x(i, s):
                sp.dma_start(x_sb[s][:], k.x_tiles[i]).then_inc(x_loaded[s], 16)

            load_x(1, 1)

            def store_packed(i):
                sp.dma_start(k.keys[bass.ds(i, 1)].rearrange("a c r -> (a c) r"), key_out[:]).then_inc(kv_stored, 16)
                sp.dma_start(k.values[bass.ds(i, 1)].rearrange("a p c -> (a p) c"), value_out[:]).then_inc(kv_stored, 16)

            def batch(i, s, after, two_after):
                one_on, two_on = (i + 1, i + 2) if isinstance(i, int) else (sp.snap(i + 1), sp.snap(i + 2))
                if not (isinstance(i, int) and i == 0):
                    sp.wait_ge(kv_copied, i)
                if after:
                    sp.dma_start(ctx_sb[1 - s][:], k.ctx_t[bass.ds(one_on, 1)].rearrange("a (t p) n -> p (a t) n", p=P)
                                 ).then_inc(ctx_loaded[1 - s], 16)
                if not (isinstance(i, int) and i == 0):
                    store_packed(i - 1)
                sp.wait_ge(q_lo, i + 1)
                for c in range(2):
                    sp.dma_start(k.q_split[bass.ds(i, 1), c].rearrange("a (t p) l -> p (a t) l", p=P),
                                 q_hl[:, :, c, :]).then_inc(q_stored, 16)
                if two_after:
                    sp.wait_ge(xn_ready, i + 1)
                    sp.dma_start(x_sb[s][:], k.x_tiles[bass.ds(two_on, 1)].rearrange("a p t d -> p (a t) d")
                                 ).then_inc(x_loaded[s], 16)

            batch(0, 0, True, True)
            batch(1, 1, True, True)
            with sp.Fori(1, B // 2 - 1) as j:
                batch(2 * j, 0, True, True)
                batch(2 * j + 1, 1, True, True)
            batch(B - 2, 0, True, False)
            batch(B - 1, 1, False, False)
            sp.wait_ge(kv_copied, B)
            store_packed(B - 1)
            sp.wait_ge(q_stored, 16 * 2 * B)
            sp.wait_ge(kv_stored, 16 * 2 * B)

        @block.gpsimd
        def _(pool):
            chain = Chain(pool, pool_steps)
            g = nc.gpsimd
            g.memset(k.ident[:], 0.0)
            g.memset(k.ident_bf[:], 0.0)
            g.memset(k.before[:], 0.0)
            g.memset(eps[:], EPS)
            g.memset(key_mul[:], 1.0)
            g.memset(key_add[:], 0.0)
            g.memset(k.ones_bf[:], 1.0)
            g.iota(column[:], pattern=[[1, L]], base=0, channel_multiplier=0, allow_small_or_imprecise_dtypes=True)
            g.iota(k.expert_no[:], pattern=[[1, E]], base=0, channel_multiplier=0, allow_small_or_imprecise_dtypes=True)
            chain.then(g.iota(k.queue_at[:], pattern=[[QUEUE, E]], base=0, channel_multiplier=0,
                              allow_small_or_imprecise_dtypes=True))
            for m in (k.ident, k.ident_bf):
                g.affine_select(out=m[:], in_=m[:], compare_op=ALU.not_equal, fill=1.0, base=0,
                                pattern=[[-1, P]], channel_multiplier=1)
            g.affine_select(out=k.before[:], in_=k.ones_bf[:], compare_op=ALU.is_gt, fill=0.0, base=0,
                            pattern=[[1, P]], channel_multiplier=-1)
            g.affine_select(out=key_mul[:], in_=key_mul[:], compare_op=ALU.not_equal, fill=FAR, base=-ROW_PAD,
                            pattern=[[0, 1]], channel_multiplier=1)
            g.affine_select(out=key_add[:], in_=key_add[:], compare_op=ALU.not_equal, fill=-FAR, base=-ROW_PAD,
                            pattern=[[0, 1]], channel_multiplier=1).then_inc(pool_ready, 1)

            def load_piece(i, c):
                source = (w1_flat if c < 2 else w2_flat)[bass.ds(i * (D * F) + (c % 2) * P * F, P * F)]
                if c < 2:
                    pool.dma_start(w_stage[c % 2][:], source.rearrange("(p f) -> p f", f=F)).then_inc(w_loaded[c % 2], 16)
                else:
                    pool.dma_start(w_stage[c % 2][:].rearrange("p (t d) -> p t d", d=D),
                                   source.rearrange("(t p d) -> p t d", p=P, d=D)).then_inc(w_loaded[c % 2], 16)

            def body(i, s, more):
                chain.restart()
                for c in range(4):
                    pool.wait_ge(w_hi, 4 * i + c + 1)
                    hi, lo, stage = w_piece(i, c)
                    chain.then(g.tensor_tensor(lo, stage, hi, ALU.subtract))
                    if c < 2 or more:
                        load_piece(i + (c + 2) // 4, (c + 2) % 4)

            load_piece(0, 0)
            load_piece(0, 1)
            over_batches(pool, lambda i, s: None, body)

        @block.scalar
        def _(act):
            act.wait_ge(k.consts_loaded, 16 * 5)
            nc.scalar.activation(k.tanh_g[:], k.tanh_g[:], ACT.Tanh).then_inc(tanh_ready, 1)
            act.wait_ge(pool_ready, 1)

            def project(i, s, et):
                act.wait_ge(q_ready, KT * i + et + 1)
                if not (isinstance(i, int) and i < 2):
                    act.wait_ge(scores_ready, LT * (i - 1))
                nc.scalar.copy(q_t[s][:, et, :], ps_q[:, et, :]).then_inc(q_copied, 1)
                act.wait_ge(q_copied, KT * i + et + 1)
                if not (isinstance(i, int) and i == 0):
                    act.wait_ge(q_stored, 32 * i)
                nc.scalar.copy(q_hl[:, et, 0, :], q_t[s][:, et, :]).then_inc(q_hi, 1)

            def turned(i, s):
                act.wait_ge(xn_turned, i + 1)
                if not (isinstance(i, int) and i == 0):
                    act.wait_ge(q_ready, KT * i)
                for t in range(KT):
                    last = nc.scalar.copy(xn_t[:, t, :], ps_t[:, t, :])
                last.then_inc(xn_t_ready, 1)

            def deviation(i):
                act.wait_ge(stats_ready, i + 1)
                nc.scalar.activation(rstd[:], moments[:, :, 1], ACT.Sqrt, bias=eps[:, 0:1]).then_inc(std_ready, 1)

            def ahead(i, s):
                deviation(i)
                turned(i, s)
                project(i, s, 0)
                project(i, s, 1)

            def weights_hi(i, c):
                act.wait_ge(w_loaded[c % 2], 16 * (2 * i + c // 2 + 1))
                hi, lo, stage = w_piece(i, c)
                nc.scalar.copy(hi, stage).then_inc(w_hi, 1)

            def body(i, s, more):
                if more:
                    deviation(i + 1)
                weights_hi(i, 0)
                weights_hi(i, 1)
                if more:
                    turned(i + 1, 1 - s)
                    project(i + 1, 1 - s, 0)
                weights_hi(i, 2)
                if more:
                    project(i + 1, 1 - s, 1)
                act.wait_ge(packed, i + 1)
                if not (isinstance(i, int) and i == 0):
                    act.wait_ge(kv_stored, 32 * i)
                nc.scalar.activation(key_out[:], ps_k[0:STACK, :],
                                     ACT.Identity, bias=key_add[:, 0:1], scale=key_mul[:, 0:1])
                nc.scalar.copy(value_out[:].rearrange("p (t c) -> p t c", t=LT), ps_v).then_inc(kv_copied, 1)
                weights_hi(i, 3)

            over_batches(act, ahead, body)

        @block.vector
        def _(dve):
            v = nc.vector
            chain = Chain(dve, steps)
            v.memset(k.n_queued[:], 0.0)
            v.memset(offset[:], 0.0)
            v.memset(k.ones_f[:], 1.0)
            chain.then(v.memset(key_cols[:, :, ROW_PAD:STACK], 0.0))
            chain.step(v.memset(key_cols[:, :, ROW_PAD:ROW_PAD + 1], 1.0))
            chain.then(v.memset(key_cols[:, :, ROW_MAX:STACK], 1.0))
            dve.wait_ge(pool_ready, 1)

            def ahead(i, s):
                dve.wait_ge(x_loaded[s], 16 * loads(i, s))
                for t in range(LT):
                    last = v.bn_stats(stats[:, t, :], x_sb[s][:, t, :])
                chain.then(last)
                for t in range(LT):
                    last = v.bn_aggr(moments[:, t, :], stats[:, t, :])
                last.then_inc(stats_ready, 1)
                dve.wait_ge(std_ready, i + 1)
                chain.then(v.reciprocal(rstd[:], rstd[:]))
                if not (isinstance(i, int) and i == 0):
                    dve.wait_ge(xn_turned, i)
                for t in range(LT):
                    last = v.tensor_scalar(xn[:, t, :], x_sb[s][:, t, :], moments[:, t, 0:1], rstd[:, t:t + 1],
                                           ALU.subtract, ALU.mult)
                last.then_inc(xn_ready, 1)

            def query_lo(i, s):
                dve.wait_ge(q_hi, KT * (i + 1))
                v.tensor_tensor(q_hl[:, :, 1, :], q_t[s][:], q_hl[:, :, 0, :], ALU.subtract).then_inc(q_lo, 1)

            def one_hot(i, t):
                dve.wait_ge(scores_read, LT * i + t + 1)
                chain.then(v.tensor_copy(best[:, t:t + 1], top8_at[:, t, 0:1]))
                v.tensor_scalar(chosen[:, t, :], column[:], best[:, t:t + 1], None, ALU.is_equal).then_inc(chosen_ready, 1)

            def body(i, s, more):
                chain.restart()
                if more:
                    ahead(i + 1, 1 - s)
                dve.wait_ge(kv_ready, i + 1)
                chain.then(v.tensor_copy(kv[:], ps_kv))
                chain.step(v.tensor_copy(key_cols[:, :, 0:DH], kv[:, :, 0:DH]))
                chain.then(v.tensor_copy(key_cols[:, :, DH:2 * DH], kv[:, :, 0:DH]))
                for t in range(LT):
                    dve.wait_ge(scores_ready, LT * i + t + 1)
                    if t == 0:
                        chain.step(v.tensor_tensor(key_cols[:, :, 2 * DH:3 * DH], kv[:, :, 0:DH],
                                                   key_cols[:, :, 0:DH], ALU.subtract))
                    else:
                        one_hot(i, t - 1)
                    chain.then(v.max(top8[:, t, :], ps_s[t % 2][:]))
                    v.max_index(top8_at[:, t, :], top8[:, t, :], ps_s[t % 2][:]).then_inc(scores_read, 1)
                one_hot(i, LT - 1)
                dve.wait_ge(counts_ready, i + 1)
                chain.then(v.tensor_copy(count[:], ps_count))
                v.tensor_scalar(used[:], count[:], 1.0, None, ALU.min).then_inc(used_ready, 1)
                chain.step(v.tensor_tensor(value_f[:, :, 0:DH], kv[:, :, DH:2 * DH],
                                           count[:, :, None].to_broadcast([P, LT, DH]), ALU.mult))
                chain.step(v.tensor_copy(value_f[:, :, DH:V1], count[:, :, None]))
                dve.wait_ge(used_ready, i + 1)
                chain.then(v.tensor_scalar(unused[:], used[:], -2.0 * L, 2.0 * L, ALU.mult, ALU.add))
                dve.wait_ge(ranks_ready, i + 1)
                chain.step(v.tensor_tensor(position[:], ps_rank, unused[:], ALU.add))
                chain.then(v.tensor_copy(total[:], ps_total))
                chain.then(v.tensor_tensor_scan(offset[:, 1:LT + 1], k.ones_f[:, 0:LT], total[:], 0.0, ALU.mult, ALU.add))
                chain.then(v.tensor_tensor(position[:], position[:], offset[:, 0:LT], ALU.add))
                for t in range(LT):
                    last = v.tensor_scalar(place[:, t, :], column[:], position[:, t:t + 1], None, ALU.is_equal)
                chain.then(v.tensor_copy(value_cols[:, :, 0:V1], value_f[:]))
                v.tensor_tensor(value_cols[:, :, V1:2 * V1], value_f[:], value_cols[:, :, 0:V1],
                                ALU.subtract).then_inc(place_ready, 1)
                if more:
                    query_lo(i + 1, 1 - s)
                dve.wait_ge(place_ready, i + 1)
                chain.step(v.tensor_copy(k.n_chosen[:, bass.ds(i, 1)], offset[:, LT:LT + 1]))

            def first(i, s):
                ahead(i, s)
                query_lo(i, s)

            def loads(i, s):
                return i // 2 + 1 if isinstance(i, int) else i_loads[0]

            i_loads = [None]
            first(0, 0)
            body(0, 0, True)
            body(1, 1, True)
            with dve.Fori(1, B // 2 - 1) as j:
                i_loads[0] = j + 1
                body(2 * j, 0, True)
                i_loads[0] = j + 2
                body(2 * j + 1, 1, True)
            body(B - 2, 0, True)
            body(B - 1, 1, False)
            chain.settle()
            chain.then(v.tensor_reduce(most[:], k.n_chosen[:], AX.X, ALU.max))
            chain.then(v.tensor_scalar(k.wide[:], most[0:1, :], float(L // 2), None, ALU.is_gt))

        @block.tensor
        def _(pe):
            t_ = nc.tensor
            pe.wait_ge(pool_ready, 1)
            pe.wait_ge(k.consts_loaded, 16 * 5)

            def turn_xn(i):
                pe.wait_ge(xn_ready, i + 1)
                if not (isinstance(i, int) and i == 0):
                    pe.wait_ge(xn_t_ready, i)
                for kt in range(KT):
                    for t in range(LT):
                        last = t_.transpose(ps_t[:, kt, t * P:(t + 1) * P], xn[:, t, kt * P:(kt + 1) * P], k.ident[:])
                last.then_inc(xn_turned, 1)

            def project(i, et):
                pe.wait_ge(xn_t_ready, i + 1)
                if not (isinstance(i, int) and i == 0):
                    pe.wait_ge(q_copied, KT * (i - 1) + et + 1)
                for kt in range(KT):
                    last = t_.matmul(ps_q[:, et, :], wq_sb[:, kt, et * P:(et + 1) * P], xn_t[:, kt, :],
                                     start=(kt == 0), stop=(kt == KT - 1))
                last.then_inc(q_ready, 1)

            KV_AT, TURN_AT = 0, 1

            def keys_and_values(i, s):
                if not (isinstance(i, int) and i == 0):
                    pe.wait_ge(kv_copied, i)
                for t in range(LT):
                    for kt in range(KT):
                        last = t_.matmul(ps_kv[:, t, :], ctx_sb[s][:, kt, t * P:(t + 1) * P], wkv_sb[:, kt, :],
                                         start=(kt == 0), stop=(kt == KT - 1))
                last.then_inc(kv_ready, 1)

            def body(i, s, more, n_loads):
                pe.wait_ge(ctx_loaded[s], 16 * n_loads)
                pe.wait_ge(q_copied, KT * (i + 1))
                for t in range(LT):
                    if not (isinstance(i, int) and i == 0 and t < 2):
                        pe.wait_ge(scores_read, LT * i + t - 1)
                    for kt in range(KT):
                        last = t_.matmul(ps_s[t % 2][:], q_t[s][:, kt, t * P:(t + 1) * P], ctx_sb[s][:, kt, :],
                                         start=(kt == 0), stop=(kt == KT - 1))
                    last.then_inc(scores_ready, 1)
                    if t == KV_AT:
                        keys_and_values(i, s)
                    if more and t == TURN_AT:
                        turn_xn(i + 1)
                if more:
                    project(i + 1, 0)
                pe.wait_ge(chosen_ready, LT * (i + 1))
                for n in range(LT):
                    for t in range(LT):
                        last = t_.matmul(ps_count[:, n:n + 1], chosen[:, t, n * P:(n + 1) * P], k.ones_bf[:, 0:1],
                                         start=(t == 0), stop=(t == LT - 1))
                last.then_inc(counts_ready, 1)
                pe.wait_ge(used_ready, i + 1)
                t_.matmul(ps_rank, k.before[:], used[:], start=True, stop=True)
                t_.matmul(ps_total, k.ones_bf[:], used[:], start=True, stop=True).then_inc(ranks_ready, 1)
                if more:
                    project(i + 1, 1)
                pe.wait_ge(place_ready, i + 1)
                for n in range(LT):
                    t_.matmul(ps_k[0:STACK, :], key_cols[:, n, :], place[:, n, :], start=(n == 0), stop=(n == LT - 1))
                for r in range(LT):
                    for n in range(LT):
                        last = t_.matmul(ps_v[:, r, :], place[:, n, r * P:(r + 1) * P], value_cols[:, n, :],
                                         start=(n == 0), stop=(n == LT - 1))
                last.then_inc(packed, 1)

            turn_xn(0)
            project(0, 0)
            project(0, 1)
            body(0, 0, True, 1)
            body(1, 1, True, 1)
            with pe.Fori(1, B // 2 - 1) as j:
                body(2 * j, 0, True, j + 1)
                body(2 * j + 1, 1, True, j + 1)
            body(B - 2, 0, True, B // 2)
            body(B - 1, 1, False, B // 2)


def attend(nc, k, sem, sb, ps):
    with ExitStack() as own:
        q_st = [sb(own, f"q_st{s}", [STACK, H, L], BF16) for s in range(2)]
        k_st = [sb(own, f"k_st{s}", [STACK, L], BF16) for s in range(2)]
        v_st = [sb(own, f"v_st{s}", [P, LT, 2 * V1], BF16) for s in range(2)]
        prob = [sb(own, f"prob{s}", [P, 2, L]) for s in range(2)]
        prob_hi = [sb(own, f"prob_hi{s}", [P, 2, L], BF16) for s in range(4)]
        prob_lo = [sb(own, f"prob_lo{s}", [P, 2, L], BF16) for s in range(4)]
        row_max = sb(own, "row_max", [P, LT, H])
        max_split = sb(own, "max_split", [P, LT, 2, H], BF16)
        max_t = sb(own, "max_t", [2 * H, L], BF16)
        heads = sb(own, "heads", [P, LT, D])
        turned = sb(own, "turned", [P, KT, L])
        inverse = sb(own, "inverse", [P, 4, LT, 1])
        rows = sb(own, "rows", [P, LT, ROW])
        x1 = rows[:, :, 0:D]
        eps = sb(own, "attend_eps", [P, 1])
        stats, moments = sb(own, "stats2", [P, LT, 6]), sb(own, "moments2", [P, LT, 2])
        rstd = sb(own, "rstd2", [P, LT])
        gate = sb(own, "gate", [P, LT, E])
        top, top_at = sb(own, "top", [P, LT, 8]), sb(own, "top_at", [P, LT, 8], U32)
        choice = sb(own, "choice", [P, LT, 2])
        gap, ratio, share = sb(own, "gap", [P, LT]), sb(own, "ratio", [P, LT]), sb(own, "share", [P, LT])
        is_choice = sb(own, "is_choice", [P, LT, 2, E])
        either = sb(own, "either", [P, LT, E], BF16)
        queue_end = sb(own, "queue_end", [P, LT, E])
        slot_taken = sb(own, "slot_taken", [P, LT, 2])
        slot_f, slot = sb(own, "slot_f", [P, LT, 2]), sb(own, "slot", [P, LT, 2], I32)
        token = sb(own, "token", [P, LT])

        ps_b = [ps(own, f"ps_b{s}", [P, L]) for s in range(2)]
        ps_a = [ps(own, f"ps_a{s}", [P, L]) for s in range(2)]
        ps_o = [ps(own, f"ps_o{s}", [P, L]) for s in range(2)]
        ps_e = [ps(own, f"ps_e{s}", [P, L]) for s in range(2)]
        ps_max = ps_e[0][:, 0:L // 2].bitcast(BF16)
        ps_gate = ps_e[0][:, 0:LT * E]
        ps_rank, ps_tile = ps_e[1][:, 0:LT * E], ps_e[1][:, LT * E:2 * LT * E]

        sems = {nt: AttendSemaphores(sem, nt) for nt in (2, 4)}
        q_loaded_w = {w: [sem(f"q_loaded{s}_{w}") for s in range(2)] for w in (2, 4)}

        v_loaded_w = {w: [sem(f"v_loaded{s}_{w}") for s in range(2)] for w in (2, 4)}

        def engine_program(which, engine):
            flag = engine.value_load(k.wide[0:1, 0:1], min_val=0, max_val=1)
            with engine.If(flag > 0):
                which(engine, 4, sems[4], q_loaded_w[4], v_loaded_w[4])
            with engine.Else():
                which(engine, 2, sems[2], q_loaded_w[2], v_loaded_w[2])

        def over_batches(engine, before_all, body, after_all):
            before_all()
            body(0, 0, True, False)
            with engine.Fori(0, B // 2 - 1) as j:
                body(2 * j + 1, 1, True, True)
                body(2 * j + 2, 0, True, True)
            body(B - 1, 1, False, True)
            after_all()

        TAKE_LAST_HEADS = 2
        PE_TURN_HEADS, PE_PROJECT, PE_TURN_ROWS, PE_GATE, PE_RANK = 2, (4, 5, 6, 7), 10, 12, 13
        ACT_COPY_HEADS, ACT_DEVIATION, ACT_COPY_ROWS, ACT_RATIO = 3, 9, 11, 13
        DVE_RESIDUAL, DVE_NORMALISE, DVE_CHOOSE, DVE_SHARES, DVE_PLACE = 8, 9, 12, 13, 14
        POOL_SCATTER = {15: range(2 * LT)}
        MAX_FIRST, MAX_HEADS, DVE_SPLIT_MAX, PE_TURN_MAX, DVE_COPY_MAX = 2, 11, 12, 13, 13
        DVE_HEADS = (0, 1, 13, 14, 15)
        POOL_HEADS = tuple(h for h in range(H) if h not in DVE_HEADS)
        LAG = 3

        def sizes(nt):
            units = nt // 2
            per_tile = 4 // nt
            tiles = LT * H // per_tile
            return units, per_tile, tiles

        def max_tiles(h, nt, half):
            units, _, tiles = sizes(nt)
            each = -(-tiles // (MAX_HEADS * units))
            n = (h - MAX_FIRST) * units + half
            if n < 0:
                return ()
            return range(min(n * each, tiles), min((n + 1) * each, tiles))

        def split_probs(engine, ops, m, b, h, half, units, heads_of, done):
            if h not in heads_of:
                return
            n = h * units + half
            u = b * H * units + n
            engine.wait_ge(m.prob_hi_ready, u + 1)
            if not (isinstance(b, int) and b == 0 and n < 4):
                engine.wait_ge(m.pv_done, u - 3)
            ops.tensor_tensor(prob_lo[n % 4][:], prob[n % 2][:], prob_hi[n % 4][:], ALU.subtract).then_inc(done, 1)

        def prob_lo_ready(m, b, n, units):
            h = n // units
            heads_of, done = (DVE_HEADS, m.prob_lo_dve) if h in DVE_HEADS else (POOL_HEADS, m.prob_lo_pool)
            return done, b * len(heads_of) * units + heads_of.index(h) * units + n % units + 1

        def sync_program(sp, nt, m, q_loaded, v_loaded):
            def load_queries(b, s):
                for c, part in enumerate((0, 1, 0)):
                    sp.dma_start(q_st[s][c * DH:(c + 1) * DH],
                                 k.q_split[bass.ds(b, 1), part].rearrange("a (h r) l -> (a r) h l", h=H)
                                 ).then_inc(q_loaded[s], 16)
                sp.dma_start(k_st[s][:], k.keys[bass.ds(b, 1)].rearrange("a c r -> (a c) r")).then_inc(q_loaded[s], 16)

            def load_values(b, s):
                sp.dma_start(v_st[s][:], k.values[bass.ds(b, 1)].rearrange("a p (t c) -> (a p) t c", t=LT)
                             ).then_inc(v_loaded[s], 16)

            def before_all():
                for s in range(2):
                    sp.wait_ge(m.stack_ones, s + 1)
                    load_queries(s, s)
                    load_values(s, s)
                sp.dma_start(x1, k.x_tiles[0]).then_inc(m.x_again, 16)
                store_max(0, 0)

            def store_max(b, s):
                sp.wait_ge(m.max_copied, b + 1)
                sp.dma_start(q_st[s][ROW_MAX:STACK], max_t[:]).then_inc(m.max_stored, 16)

            def store(e):
                sp.wait_ge(m.x1_ready, e + 1)
                sp.dma_start(k.out[bass.ds(e, 1)].rearrange("a (t p) d -> p (a t) d", p=P), x1).then_inc(m.x1_stored, 16)

            def reload(e):
                sp.wait_ge(m.scattered, 16 * 2 * LT * e)
                sp.dma_start(x1, k.x_tiles[bass.ds(e, 1)].rearrange("a p t d -> p (a t) d")).then_inc(m.x_again, 16)

            def body(b, s, more, after):
                if after and more:
                    sp.wait_ge(m.pv_done, H * (nt // 2) * b)
                    load_values(b + 1, 1 - s)
                if after:
                    store(b - 1)
                if more:
                    store_max(b + 1, 1 - s)
                if more and not (isinstance(b, int) and b == B - 2):
                    sp.wait_ge(m.logits_ready, H * nt * (b + 1))
                    load_queries(b + 2, s)
                if after:
                    reload(b)

            def after_all():
                store(B - 1)
                sp.wait_ge(m.x1_stored, 16 * B)

            before_all()
            body(0, 0, True, False)
            with sp.Fori(0, B // 2 - 2) as j:
                body(2 * j + 1, 1, True, True)
                body(2 * j + 2, 0, True, True)
            body(B - 3, 1, True, True)
            body(B - 2, 0, True, True)
            body(B - 1, 1, False, True)
            after_all()

        def pool_program(pool, nt, m, q_loaded, v_loaded):
            units, _, _ = sizes(nt)
            g = nc.gpsimd
            chain = Chain(pool, m.attend_pool_steps)

            def before_all():
                g.memset(eps[:], EPS)
                g.iota(token[:], pattern=[[P, LT]], base=-L, channel_multiplier=1,
                       allow_small_or_imprecise_dtypes=True).then_inc(m.constants2, 1)

            def scatter(e, some):
                if 0 in some:
                    pool.wait_ge(m.slots_ready, e + 1)
                    chain.then(g.tensor_tensor(slot_taken[:], slot_f[:], k.ones_f[:, 0:LT, None].to_broadcast([P, LT, 2]),
                                               ALU.mult))
                    chain.then(g.tensor_copy(slot[:], slot_taken[:]))
                for t, c in ((n // 2, n % 2) for n in some):
                    pool.indirect_dma_start(k.queue[:], bass.IndirectOffsetOnAxis(ap=slot[:, t, c:c + 1], axis=0),
                                            rows[:, t, :], None).then_inc(m.scattered, 16)

            def body(b, s, more, after):
                chain.restart()
                for h in range(H):
                    for half in range(units):
                        split_probs(pool, g, m, b, h, half, units, POOL_HEADS, m.prob_lo_pool)
                    if after and h in POOL_SCATTER:
                        scatter(b - 1, POOL_SCATTER[h])

            def after_all():
                scatter(B - 1, range(2 * LT))
                pool.wait_ge(m.scattered, 16 * 2 * LT * B)

            over_batches(pool, before_all, body, after_all)

        def scalar_program(act, nt, m, q_loaded, v_loaded):
            units, _, _ = sizes(nt)
            a = nc.scalar
            first_of = lambda b: isinstance(b, int) and b == 0

            def before_all():
                act.wait_ge(m.constants2, 1)

            def body(b, s, more, after):
                for h in range(H):
                    for half in range(units):
                        u, n = b * H * units + h * units + half, h * units + half
                        for r in range(2):
                            act.wait_ge(m.logits_ready, 2 * u + r + 1)
                            if r == 0 and not (first_of(b) and n < 2):
                                if n < 2:
                                    act.wait_ge(*prob_lo_ready(m, b - 1, n - 2 + H * units, units))
                                else:
                                    act.wait_ge(*prob_lo_ready(m, b, n - 2, units))
                            a.activation(prob[n % 2][:, r, :], ps_a[r][:], ACT.Exp, scale=SCALE).then_inc(m.exp_ready, 1)
                        if not (first_of(b) and n < 4):
                            act.wait_ge(m.pv_done, u - 3)
                        act.wait_ge(m.exp_ready, 2 * u + 2)
                        a.copy(prob_hi[n % 4][:], prob[n % 2][:]).then_inc(m.prob_hi_ready, 1)
                    if after:
                        stages(b - 1, h)

            def stages(e, h):
                if h in (ACT_COPY_HEADS, ACT_COPY_ROWS):
                    done, ready = ((m.heads_turned, m.heads_t_ready) if h == ACT_COPY_HEADS else
                                   (m.rows_turned, m.rows_t_ready))
                    act.wait_ge(done, e + 1)
                    if h == ACT_COPY_HEADS and not first_of(e):
                        act.wait_ge(m.gate_ready, e)
                    a.copy(turned[:, 0, :], ps_e[0][:])
                    a.copy(turned[:, 1, :], ps_e[1][:]).then_inc(ready, 1)
                if h == ACT_DEVIATION:
                    act.wait_ge(m.moments_ready, e + 1)
                    a.activation(rstd[:], moments[:, :, 1], ACT.Sqrt, bias=eps[:, 0:1]).then_inc(m.std2_ready, 1)
                if h == ACT_RATIO:
                    act.wait_ge(m.gap_ready, e + 1)
                    a.activation(ratio[:], gap[:], ACT.Exp).then_inc(m.ratio_ready, 1)

            def after_all():
                for h in range(H):
                    stages(B - 1, h)

            over_batches(act, before_all, body, after_all)

        def vector_program(dve, nt, m, q_loaded, v_loaded):
            units, per_tile, tiles = sizes(nt)
            v = nc.vector
            chain = Chain(dve, m.attend_steps)
            first_of = lambda b: isinstance(b, int) and b == 0

            def take_max(b, tile):
                t, group = tile // (H // per_tile), tile % (H // per_tile)
                dve.wait_ge(m.logits_b_ready, tiles * b + tile + 1)
                v.tensor_reduce(row_max[:, t, group * per_tile:(group + 1) * per_tile],
                                ps_b[tile % 2][:].rearrange("p (h r) -> p h r", h=per_tile),
                                AX.X, ALU.max).then_inc(m.max_taken, 1)

            def split_max(b):
                dve.wait_ge(m.max_taken, tiles * (b + 1))
                if not first_of(b):
                    dve.wait_ge(m.max_turned, b)
                chain.then(v.tensor_scalar(max_split[:, :, 0, :], row_max[:], -1.0, None, ALU.mult))
                v.scalar_tensor_tensor(out=max_split[:, :, 1, :], in0=row_max[:], scalar=-1.0, in1=max_split[:, :, 0, :],
                                       op0=ALU.mult, op1=ALU.subtract).then_inc(m.max_ready, 1)

            def copy_max(b):
                dve.wait_ge(m.max_turned, b + 1)
                if not first_of(b):
                    dve.wait_ge(m.max_stored, 16 * b)
                v.tensor_copy(max_t[:], ps_max[0:2 * H, :]).then_inc(m.max_copied, 1)

            def take_heads(b, group):
                dve.wait_ge(m.pv_done, H * units * b + 4 * units * (group + 1))
                sums = ps_o[group % 2][:, 0:4 * LT * V1].rearrange("p (h t c) -> p h t c", h=4, t=LT)
                if group == 0 and not first_of(b):
                    dve.wait_ge(m.heads_turned, b)
                chain.then(v.reciprocal(inverse[:], sums[:, :, :, DH:V1]))
                v.tensor_tensor(heads[:, :, group * 4 * DH:(group + 1) * 4 * DH].rearrange("p t (h c) -> p h t c", h=4),
                                sums[:, :, :, 0:DH], inverse[:].to_broadcast([P, 4, LT, DH]),
                                ALU.mult).then_inc(m.heads_ready, 1)
                dve.wait_ge(m.heads_ready, 4 * b + group + 1)

            def before_all():
                for s in range(2):
                    v.memset(q_st[s][:], 1.0).then_inc(m.stack_ones, 1)
                for tile in range(tiles):
                    take_max(0, tile)
                split_max(0)
                copy_max(0)
                dve.wait_ge(m.constants2, 1)

            def stages(e, h):
                if h == DVE_RESIDUAL:
                    dve.wait_ge(m.x_again, 16 * (e + 1))
                    dve.wait_ge(m.y_ready, e + 1)
                    for c in range(2):
                        half = x1[:, 2 * c:2 * c + 2, :]
                        last = v.scalar_tensor_tensor(out=half, in0=ps_e[c][:].rearrange("p (t d) -> p t d", t=2),
                                                      scalar=k.tanh_g[:, 0:1], in1=half, op0=ALU.mult, op1=ALU.add)
                    last.then_inc(m.x1_ready, 1)
                    dve.wait_ge(m.x1_ready, e + 1)
                    for t in range(LT):
                        last = v.bn_stats(stats[:, t, :], x1[:, t, :])
                    chain.then(last)
                    for t in range(LT):
                        last = v.bn_aggr(moments[:, t, :], stats[:, t, :])
                    last.then_inc(m.moments_ready, 1)
                if h == DVE_NORMALISE:
                    dve.wait_ge(m.std2_ready, e + 1)
                    chain.then(v.reciprocal(rstd[:], rstd[:]))
                    dve.wait_ge(m.x1_stored, 16 * (e + 1))
                    for t in range(LT):
                        last = v.tensor_scalar(rows[:, t, 0:D], x1[:, t, :], moments[:, t, 0:1], rstd[:, t:t + 1],
                                               ALU.subtract, ALU.mult)
                    last.then_inc(m.rows_ready, 1)
                if h == DVE_CHOOSE:
                    dve.wait_ge(m.gate_ready, e + 1)
                    chain.then(v.tensor_copy(gate[:], ps_gate.rearrange("p (t e) -> p t e", t=LT)))
                    for t in range(LT):
                        last = v.max(top[:, t, :], gate[:, t, :])
                    chain.then(last)
                    for t in range(LT):
                        last = v.max_index(top_at[:, t, :], top[:, t, :], gate[:, t, :])
                    chain.step(last)
                    v.tensor_tensor(gap[:], top[:, :, 1], top[:, :, 0], ALU.subtract).then_inc(m.gap_ready, 1)
                    chain.settle()
                    chain.then(v.tensor_copy(choice[:], top_at[:, :, 0:2]))
                    chain.step(v.tensor_copy(rows[:, :, D + 2], choice[:, :, 0]))
                    chain.then(v.tensor_tensor(is_choice[:], k.expert_no[:, None, None, :].to_broadcast([P, LT, 2, E]),
                                               choice[:, :, :, None].to_broadcast([P, LT, 2, E]), ALU.is_equal))
                    v.tensor_tensor(either[:], is_choice[:, :, 0, :], is_choice[:, :, 1, :], ALU.add).then_inc(m.either_ready, 1)
                if h == DVE_SHARES:
                    dve.wait_ge(m.ratio_ready, e + 1)
                    chain.step(v.tensor_copy(rows[:, :, D + 3], token[:]))
                    chain.then(v.tensor_scalar(share[:], ratio[:], 1.0, None, ALU.add))
                    chain.then(v.reciprocal(share[:], share[:]))
                    chain.then(v.tensor_scalar(share[:], share[:], k.tanh_g[:, 1:2], None, ALU.mult))
                    chain.step(v.tensor_copy(rows[:, :, D], share[:]))
                    chain.then(v.tensor_tensor(rows[:, :, D + 1], share[:], ratio[:], ALU.mult))
                if h == DVE_PLACE:
                    dve.wait_ge(m.ranked, e + 1)
                    tile_sums = ps_tile.rearrange("p (t e) -> p t e", t=LT)
                    chain.then(v.tensor_tensor(queue_end[:, 0, :], k.n_queued[:], k.queue_at[:], ALU.add))
                    for t in range(LT):
                        if t + 1 < LT:
                            chain.step(v.tensor_tensor(queue_end[:, t + 1, :], queue_end[:, t, :], tile_sums[:, t, :], ALU.add))
                        chain.then(v.tensor_tensor(k.n_queued[:], k.n_queued[:], tile_sums[:, t, :], ALU.add))
                    chain.then(v.tensor_tensor(queue_end[:], queue_end[:], ps_rank.rearrange("p (t e) -> p t e", t=LT), ALU.add))
                    chain.then(v.tensor_tensor(is_choice[:], is_choice[:], queue_end[:, :, None, :].to_broadcast([P, LT, 2, E]), ALU.mult))
                    v.tensor_reduce(slot_f[:], is_choice[:], AX.X, ALU.add).then_inc(m.slots_ready, 1)
                    dve.wait_ge(m.slots_ready, e + 1)

            def body(b, s, more, after):
                for h in range(H):
                    for half in range(units):
                        if more:
                            for tile in max_tiles(h, nt, half):
                                take_max(b + 1, tile)
                        split_probs(dve, v, m, b, h, half, units, DVE_HEADS, m.prob_lo_dve)
                    if after and h == TAKE_LAST_HEADS:
                        take_heads(b - 1, 3)
                    if h > 4 and (h - TAKE_LAST_HEADS) % 4 == 0:
                        take_heads(b, (h - TAKE_LAST_HEADS) // 4 - 1)
                    if after:
                        stages(b - 1, h)
                    if more and h == DVE_SPLIT_MAX:
                        split_max(b + 1)
                    if more and h == DVE_COPY_MAX:
                        copy_max(b + 1)
                chain.then(v.tensor_scalar(token[:], token[:], float(L), None, ALU.add))
                chain.restart()

            def after_all():
                take_heads(B - 1, 3)
                for h in range(H):
                    stages(B - 1, h)
                chain.settle()

            over_batches(dve, before_all, body, after_all)

        def tensor_program(pe, nt, m, q_loaded, v_loaded):
            units, per_tile, tiles = sizes(nt)
            t_ = nc.tensor
            first_of = lambda b: isinstance(b, int) and b == 0
            width = nt * P

            def logits_b(b, s, tile):
                t, group = tile // (H // per_tile), tile % (H // per_tile)
                if not (first_of(b) and tile < 2):
                    pe.wait_ge(m.max_taken, tiles * b + tile - 1)
                for i in range(per_tile):
                    last = t_.matmul(ps_b[tile % 2][:, i * width:(i + 1) * width],
                                     q_st[s][0:ROW_MAX, group * per_tile + i, t * P:(t + 1) * P],
                                     k_st[s][0:ROW_MAX, 0:width], start=True, stop=True)
                last.then_inc(m.logits_b_ready, 1)

            def turn_max(b):
                pe.wait_ge(m.max_ready, b + 1)
                for t in range(LT):
                    last = t_.transpose(ps_max[0:2 * H, t * P:(t + 1) * P],
                                        max_split[:, t].rearrange("p c h -> p (c h)"), k.ident_bf[:])
                last.then_inc(m.max_turned, 1)

            def logits(b, s, h, half):
                u, n = b * H * units + h * units + half, h * units + half
                for r in range(2):
                    if not (first_of(b) and n == 0):
                        pe.wait_ge(m.exp_ready, 2 * u + r - 1)
                    key_tile = 2 * half + r
                    t_.matmul(ps_a[r][:], k_st[s][:, key_tile * P:(key_tile + 1) * P], q_st[s][:, h, :],
                              start=True, stop=True).then_inc(m.logits_ready, 1)

            def weighted(b, s, n, own_loads):
                h, half = n // units, n % units
                group, i = h // 4, h % 4
                if i == 0 and half == 0 and not (first_of(b) and group < 2):
                    pe.wait_ge(m.heads_ready, 4 * b + group - 1)
                if n == 0:
                    pe.wait_ge(v_loaded[s], 16 * own_loads)
                pe.wait_ge(*prob_lo_ready(m, b, n, units))
                for t in range(LT):
                    at = (i * LT + t) * V1
                    for r in range(2):
                        key_tile = 2 * half + r
                        for c, (weights, col) in enumerate(((prob_hi, 0), (prob_hi, V1), (prob_lo, 0))):
                            last = t_.matmul(ps_o[group % 2][:, at:at + V1], weights[n % 4][:, r, t * P:(t + 1) * P],
                                             v_st[s][:, key_tile, col:col + V1],
                                             start=(i == 0 and half == 0 and t == 0 and r == 0 and c == 0),
                                             stop=(i == 3 and half == units - 1 and t == LT - 1 and r == 1 and c == 2),
                                             skip_group_check=True)
                last.then_inc(m.pv_done, 1)

            def stages(e, h):
                if h == PE_TURN_HEADS:
                    pe.wait_ge(m.heads_ready, 4 * (e + 1))
                    if not first_of(e):
                        pe.wait_ge(m.slots_ready, e)
                    turn(heads, m.heads_turned)
                if h in PE_PROJECT:
                    t = PE_PROJECT.index(h)
                    if t == 0:
                        pe.wait_ge(m.heads_t_ready, e + 1)
                    for kt in range(KT):
                        last = t_.matmul(ps_e[t // 2][:, (t % 2) * D:(t % 2 + 1) * D], turned[:, kt, t * P:(t + 1) * P],
                                         k.wc_sb[:, kt, :], start=(kt == 0), stop=(kt == KT - 1))
                    if t == LT - 1:
                        last.then_inc(m.y_ready, 1)
                if h == PE_TURN_ROWS:
                    pe.wait_ge(m.rows_ready, e + 1)
                    turn(rows, m.rows_turned)
                if h == PE_GATE:
                    pe.wait_ge(m.rows_t_ready, e + 1)
                    for t in range(LT):
                        for kt in range(KT):
                            last = t_.matmul(ps_gate[:, t * E:(t + 1) * E], turned[:, kt, t * P:(t + 1) * P],
                                             k.gate_sb[:, kt, :], start=(kt == 0), stop=(kt == KT - 1))
                    last.then_inc(m.gate_ready, 1)
                if h == PE_RANK:
                    pe.wait_ge(m.either_ready, e + 1)
                    both = either[:].rearrange("p t e -> p (t e)")
                    t_.matmul(ps_rank, k.before[:], both, start=True, stop=True)
                    t_.matmul(ps_tile, k.ones_bf[:], both, start=True, stop=True).then_inc(m.ranked, 1)

            def turn(source, done):
                for kt in range(KT):
                    for t in range(LT):
                        last = t_.transpose(ps_e[kt][:, t * P:(t + 1) * P], source[:, t, kt * P:(kt + 1) * P], k.ident[:])
                last.then_inc(done, 1)

            def before_all():
                pe.wait_ge(q_loaded[0], 64)
                for tile in range(tiles):
                    logits_b(0, 0, tile)
                turn_max(0)

            def body(b, s, more, after, own_loads, next_loads):
                pe.wait_ge(m.max_stored, 16 * (b + 1))
                for h in range(H):
                    if more and h == MAX_FIRST:
                        pe.wait_ge(q_loaded[1 - s], 64 * next_loads)
                    for half in range(units):
                        n = h * units + half
                        spread = max_tiles(h, nt, half) if more else ()
                        for tile in spread[0:1]:
                            logits_b(b + 1, 1 - s, tile)
                        logits(b, s, h, half)
                        for tile in spread[1:2]:
                            logits_b(b + 1, 1 - s, tile)
                        if n >= LAG:
                            weighted(b, s, n - LAG, own_loads)
                        elif after:
                            weighted(b - 1, 1 - s, H * units + n - LAG, None)
                        for tile in spread[2:]:
                            logits_b(b + 1, 1 - s, tile)
                    if after:
                        stages(b - 1, h)
                    if more and h == PE_TURN_MAX:
                        turn_max(b + 1)

            def after_all():
                for n in range(H * units - LAG, H * units):
                    weighted(B - 1, 1, n, None)
                for h in range(H):
                    stages(B - 1, h)

            before_all()
            body(0, 0, True, False, 1, 1)
            with pe.Fori(0, B // 2 - 1) as j:
                body(2 * j + 1, 1, True, True, j + 1, j + 2)
                body(2 * j + 2, 0, True, True, j + 2, j + 2)
            body(B - 1, 1, False, True, B // 2, None)
            after_all()

        block = own.enter_context(nc.Block())

        @block.sync
        def _(sp):
            engine_program(sync_program, sp)

        @block.gpsimd
        def _(pool):
            engine_program(pool_program, pool)

        @block.scalar
        def _(act):
            engine_program(scalar_program, act)

        @block.vector
        def _(dve):
            engine_program(vector_program, dve)

        @block.tensor
        def _(pe):
            engine_program(tensor_program, pe)


def experts(nc, k, sem, sb, ps):
    with ExitStack() as own:
        full = sb(own, "full", [P, E, QUEUE // TILE])
        thresholds = sb(own, "thresholds", [P, QUEUE // TILE])
        tile_no = sb(own, "tile_no", [P, N_TILES])
        needed, end, start = (sb(own, n, [P, E]) for n in ("needed", "tiles_end", "tiles_start"))
        ones_e = sb(own, "ones_e", [P, E])
        mine, past = sb(own, "mine", [P, N_TILES, E]), sb(own, "past", [P, N_TILES, E])
        valid, first_row = sb(own, "valid", [P, N_TILES]), sb(own, "first_row", [P, N_TILES])
        tile_expert = sb(own, "tile_expert", [P, N_TILES])
        row_of = sb(own, "row_of", [P, N_TILES], I32)
        expert_of = sb(own, "expert_of", [P, N_TILES], I32)
        pad_f = sb(own, "pad_f", [P, E + 1])
        pad_at = sb(own, "pad_at", [P, E + 1], I32)

        padding = sb(own, "padding", [P, 2, ROW])
        b1_sb = sb(own, "b1_sb", [P, E, FC])
        b2_two = sb(own, "b2_two", [2, E * D])
        b2_first = sb(own, "b2_first", [2, E * D], BF16)
        b2_split = sb(own, "b2_split", [2, E, D], BF16)
        minus_row = sb(own, "minus_row", [2, 1])

        xg = [sb(own, f"xg{s}", [P, 2, ROW]) for s in range(2)]
        tails = sb(own, "tails", [P, N_TILES, 2, 4])
        weight = sb(own, "weight", [P, N_TILES, 2])
        part_a, part_b = sb(own, "part_a", [P, 2]), sb(own, "part_b", [P, 2])
        bias = [sb(own, f"bias{s}", [P, FC]) for s in range(2)]
        x_hi = [sb(own, f"x_hi{s}", [P, KT, TILE], BF16) for s in range(2)]
        x_lo = [sb(own, f"x_lo{s}", [P, KT, TILE], BF16) for s in range(2)]
        hidden = sb(own, "hidden", [P, FC, TILE])
        h_hi = [sb(own, f"h_hi{s}", [P, FC, TILE], BF16) for s in range(2)]
        h_lo = [sb(own, f"h_lo{s}", [P, FC, TILE], BF16) for s in range(2)]
        y = [sb(own, f"y{s}", [P, 2, D]) for s in range(2)]
        token_f, token_at = sb(own, "token_f", [P, 2]), sb(own, "token_at", [P, 2], I32)

        ps_x = ps(own, "ps_x", [P, KT, TILE])
        ps_h = [ps(own, f"ps_h{n}", [P, 2, TILE]) for n in range(FC // 2)]
        ps_y = [ps(own, f"ps_y{s}", [P, 2, D]) for s in range(2)]

        bias_loaded, tables_ready, scheduled = sem("bias_loaded"), sem("tables_ready"), sem("scheduled")
        padded, x_turned = sem("padded"), sem("x_turned")
        row_loaded = [sem(f"row_loaded{s}") for s in range(2)]
        tail_taken, x_hi_ready, x_lo_ready = sem("tail_taken"), sem("x_hi_ready"), sem("x_lo_ready")
        h_ready, gelu_done, h_hi_ready, h_lo_ready = (sem("h_ready"), sem("gelu_done"), sem("h_hi_ready"),
                                                      sem("h_lo_ready"))
        y_summed, y_weighted, added = sem("y_summed"), sem("y_weighted"), sem("added")
        dve_steps, pool_steps = sem("experts_steps"), sem("experts_pool_steps")
        PAIRS = FC // 2

        block = own.enter_context(nc.Block())

        def over_tiles(engine, body):
            body(0, 0, 0, True, True)
            body(1, 0, 1, True, True)
            with engine.Fori(1, (N_TILES - 3) // 2) as j:
                body(2 * j, j, 0, True, True)
                body(2 * j + 1, j, 1, True, True)
            for i in range(2 * ((N_TILES - 3) // 2), N_TILES):
                body(i, i // 2, i % 2, i + 1 < N_TILES, i + 2 < N_TILES)

        def first(i, n=1):
            return isinstance(i, int) and i < n

        def load_expert(engine, i):
            return engine.value_load(expert_of[0:1, bass.ds(i, 1)], min_val=0, max_val=E - 1)

        @block.sync
        def _(sp):
            sp.dma_start(b1_sb[:], k.b1_t).then_inc(bias_loaded, 16)
            sp.dma_start(b2_two[:], k.b2.rearrange("e d -> (e d)")[None, :].to_broadcast([2, E * D])).then_inc(bias_loaded, 16)
            sp.wait_ge(scheduled, 1)
            pads = [sp.value_load(pad_at[0:1, n:n + 1], min_val=0, max_val=DUMMY) for n in range(E + 1)]
            for at in pads:
                sp.dma_start(k.queue[bass.ds(at, TILE)].rearrange("(s p) c -> p s c", p=P), padding[:]).then_inc(padded, 16)
            sp.wait_ge(padded, 16 * (E + 1))

            def load(i, s):
                row = sp.value_load(row_of[0:1, bass.ds(i, 1)], min_val=0, max_val=DUMMY)
                sp.dma_start(xg[s][:], k.queue[bass.ds(row, TILE)].rearrange("(s p) c -> p s c", p=P)).then_inc(row_loaded[s], 16)

            def body(i, half, s, more, two_more):
                if two_more:
                    sp.wait_ge(x_turned, i + 1)
                    sp.wait_ge(tail_taken, i + 1)
                    load(i + 2, s)

            load(0, 0)
            load(1, 1)
            over_tiles(sp, body)

        @block.gpsimd
        def _(pool):
            g = nc.gpsimd
            chain = Chain(pool, pool_steps)
            exact = dict(allow_small_or_imprecise_dtypes=True)
            g.iota(thresholds[:], pattern=[[TILE, QUEUE // TILE]], base=0, channel_multiplier=0, **exact)
            g.iota(tile_no[:], pattern=[[1, N_TILES]], base=0, channel_multiplier=0, **exact)
            g.iota(minus_row[:], pattern=[[0, 1]], base=0, channel_multiplier=-1, **exact)
            g.memset(ones_e[:], 1.0).then_inc(tables_ready, 1)

            def body(i, half, s, more, two_more):
                if not first(i):
                    pool.wait_ge(added, 32 * i)
                pool.wait_ge(y_weighted, i + 1)
                chain.then(g.tensor_tensor(token_f[:], tails[:, bass.ds(i, 1), :, 3].rearrange("p a s -> p (a s)"),
                                           k.ones_f[:, 0:2], ALU.mult))
                chain.then(g.tensor_copy(token_at[:], token_f[:]))
                for t in range(2):
                    pool.indirect_dma_start(k.out_rows, bass.IndirectOffsetOnAxis(ap=token_at[:, t:t + 1], axis=0),
                                            y[s][:, t, :], None, bounds_check=B * L - 1, oob_is_err=False,
                                            compute_op=ALU.add).then_inc(added, 16)
                chain.restart()

            over_tiles(pool, body)
            pool.wait_ge(added, 32 * N_TILES)

        @block.scalar
        def _(act):
            a = nc.scalar

            def split_x(i, s):
                act.wait_ge(x_turned, i + 1)
                a.copy(x_hi[s][:], ps_x[:]).then_inc(x_hi_ready, 1)

            def body(i, half, s, more, two_more):
                if more:
                    split_x(i + 1, 1 - s)
                for n in range(PAIRS):
                    if not first(i):
                        act.wait_ge(h_lo_ready, PAIRS * (i - 1) + n + 1)
                    act.wait_ge(h_ready, PAIRS * i + n + 1)
                    for c in range(2):
                        f = 2 * n + c
                        last = a.activation(hidden[:, f, :], ps_h[n][:, c, :], ACT.Gelu, bias=bias[s][:, f:f + 1])
                    last.then_inc(gelu_done, 1)
                    act.wait_ge(gelu_done, PAIRS * i + n + 1)
                    a.copy(h_hi[s][:, 2 * n:2 * n + 2, :], hidden[:, 2 * n:2 * n + 2, :]).then_inc(h_hi_ready, 1)

            split_x(0, 0)
            over_tiles(act, body)

        @block.vector
        def _(dve):
            v = nc.vector
            chain = Chain(dve, dve_steps)
            every = lambda a: a[:, None, :].to_broadcast([P, N_TILES, E])
            each = lambda a: a[:, :, None].to_broadcast([P, N_TILES, E])
            chain.step(v.memset(padding[:], 0.0))
            dve.wait_ge(tables_ready, 1)
            chain.then(v.tensor_tensor(full[:], k.n_queued[:, :, None].to_broadcast([P, E, QUEUE // TILE]),
                                       thresholds[:, None, :].to_broadcast([P, E, QUEUE // TILE]), ALU.is_gt))
            chain.step(v.memset(padding[:, :, D + 3:ROW], NO_TOKEN))
            chain.step(v.tensor_tensor(pad_f[:, 0:E], k.queue_at[:], k.n_queued[:], ALU.add))
            chain.step(v.memset(pad_f[:, E:E + 1], float(DUMMY)))
            chain.then(v.tensor_reduce(needed[:], full[:], AX.X, ALU.add))
            chain.step(v.tensor_copy(pad_at[:], pad_f[:]))
            chain.then(v.tensor_tensor_scan(end[:], ones_e[:], needed[:], 0.0, ALU.mult, ALU.add))
            chain.then(v.tensor_tensor(start[:], end[:], needed[:], ALU.subtract))
            chain.step(v.tensor_tensor(mine[:], each(tile_no), every(start), ALU.is_ge))
            chain.then(v.tensor_tensor(past[:], each(tile_no), every(end), ALU.is_ge))
            chain.then(v.tensor_tensor(mine[:], mine[:], past[:], ALU.subtract))
            chain.step(v.tensor_reduce(valid[:], mine[:], AX.X, ALU.add))
            chain.then(v.tensor_tensor(past[:], mine[:], every(k.expert_no), ALU.mult))
            chain.then(v.tensor_reduce(tile_expert[:], past[:], AX.X, ALU.add))
            chain.then(v.scalar_tensor_tensor(out=start[:], in0=start[:], scalar=-float(TILE), in1=k.queue_at[:],
                                              op0=ALU.mult, op1=ALU.add))
            chain.then(v.tensor_tensor(mine[:], mine[:], every(start), ALU.mult))
            chain.step(v.tensor_reduce(first_row[:], mine[:], AX.X, ALU.add))
            chain.then(v.tensor_scalar(tile_no[:], tile_no[:], float(TILE), -float(DUMMY), ALU.mult, ALU.add))
            chain.then(v.tensor_tensor(tile_no[:], tile_no[:], valid[:], ALU.mult))
            chain.then(v.scalar_tensor_tensor(out=first_row[:], in0=first_row[:], scalar=float(DUMMY), in1=tile_no[:],
                                              op0=ALU.add, op1=ALU.add))
            chain.then(v.tensor_copy(row_of[:], first_row[:]))
            v.tensor_copy(expert_of[:], tile_expert[:]).then_inc(scheduled, 1)
            dve.wait_ge(bias_loaded, 32)
            chain.then(v.tensor_copy(b2_first[:], b2_two[:]))
            chain.step(v.scalar_tensor_tensor(out=b2_split[:].rearrange("c e d -> c (e d)"), in0=b2_first[:],
                                              scalar=minus_row[:, 0:1], in1=b2_two[:], op0=ALU.mult, op1=ALU.add))
            dve.wait_ge(scheduled, 1)

            def prepare(i, half, s):
                e = load_expert(dve, i)
                dve.wait_ge(row_loaded[s], 16 * (half + 1))
                tail = tails[:, bass.ds(i, 1)].rearrange("p a s c -> p (a s) c")
                v.tensor_copy(tail, xg[s][:, :, D:ROW]).then_inc(tail_taken, 1)
                v.tensor_copy(bias[s][:], b1_sb[:, bass.ds(e, 1), :].rearrange("p a f -> p (a f)"))
                dve.wait_ge(tail_taken, i + 1)
                this = tile_expert[:, bass.ds(i, 1)]
                chain.step(v.scalar_tensor_tensor(out=part_a[:], in0=tail[:, :, 2], scalar=this, in1=tail[:, :, 0],
                                                  op0=ALU.is_equal, op1=ALU.mult))
                chain.then(v.scalar_tensor_tensor(out=part_b[:], in0=tail[:, :, 2], scalar=this, in1=tail[:, :, 1],
                                                  op0=ALU.not_equal, op1=ALU.mult))
                chain.step(v.tensor_tensor(weight[:, bass.ds(i, 1), :].rearrange("p a s -> p (a s)"), part_a[:], part_b[:], ALU.add))
                dve.wait_ge(x_hi_ready, i + 1)
                v.tensor_tensor(x_lo[s][:], ps_x[:], x_hi[s][:], ALU.subtract).then_inc(x_lo_ready, 1)

            def finish(i, s):
                dve.wait_ge(y_summed, i + 1)
                if not first(i, 2):
                    dve.wait_ge(added, 32 * (i - 1))
                for t in range(2):
                    last = v.tensor_scalar(y[s][:, t, :], ps_y[s][:, t, :],
                                           weight[:, bass.ds(i, 1), t:t + 1].rearrange("p a s -> p (a s)"), None, ALU.mult)
                last.then_inc(y_weighted, 1)

            def body(i, half, s, more, two_more):
                chain.restart()
                if more:
                    prepare(i + 1, half + s, 1 - s)
                for n in range(PAIRS):
                    dve.wait_ge(h_hi_ready, PAIRS * i + n + 1)
                    both = slice(2 * n, 2 * n + 2)
                    v.tensor_tensor(h_lo[s][:, both, :], hidden[:, both, :], h_hi[s][:, both, :], ALU.subtract
                                    ).then_inc(h_lo_ready, 1)
                if not first(i):
                    finish(i - 1, 1 - s)

            prepare(0, 0, 0)
            over_tiles(dve, body)
            finish(N_TILES - 1, (N_TILES - 1) % 2)

        @block.tensor
        def _(pe):
            t_ = nc.tensor

            def turn(i, half, s):
                pe.wait_ge(row_loaded[s], 16 * (half + 1))
                if not first(i):
                    pe.wait_ge(x_lo_ready, i)
                for kt in range(KT):
                    for t in range(2):
                        last = t_.transpose(ps_x[:, kt, t * P:(t + 1) * P], xg[s][:, t, kt * P:(kt + 1) * P], k.ident[:])
                last.then_inc(x_turned, 1)

            def layer1(i, s):
                e = load_expert(pe, i)
                pe.wait_ge(x_lo_ready, i + 1)
                for n in range(PAIRS):
                    if not first(i):
                        pe.wait_ge(gelu_done, PAIRS * (i - 1) + n + 1)
                    for c in range(2):
                        f = slice((2 * n + c) * P, (2 * n + c + 1) * P)
                        terms = [(kt, part, xs) for kt in range(KT) for part, xs in ((0, x_hi), (0, x_lo), (1, x_hi))]
                        for q, (kt, part, xs) in enumerate(terms):
                            last = t_.matmul(ps_h[n][:, c, :],
                                             k.w1_split[:, bass.ds(e, 1), part, kt, f].rearrange("p a f -> p (a f)"),
                                             xs[s][:, kt, :], start=(q == 0), stop=(q == len(terms) - 1))
                    last.then_inc(h_ready, 1)

            def layer2(i, s):
                e = load_expert(pe, i)
                pe.wait_ge(h_lo_ready, PAIRS * (i + 1))
                if not first(i, 2):
                    pe.wait_ge(y_weighted, i - 1)
                for t in range(2):
                    token = slice(t * P, (t + 1) * P)
                    for f in range(FC):
                        for q, (hs, part) in enumerate(((h_hi, 0), (h_hi, 1), (h_lo, 0))):
                            t_.matmul(ps_y[s][:, t, :], hs[s][:, f, token],
                                      k.w2_split[:, bass.ds(e, 1), part, f, :].rearrange("p a d -> p (a d)"),
                                      start=(f == 0 and q == 0), stop=False)
                    last = t_.matmul(ps_y[s][:, t, :], k.ones_bf[0:2, :],
                                     b2_split[:, bass.ds(e, 1), :].rearrange("c a d -> c (a d)"), start=False, stop=True)
                last.then_inc(y_summed, 1)

            def body(i, half, s, more, two_more):
                if more:
                    turn(i + 1, half + s, 1 - s)
                layer1(i, s)
                if not first(i):
                    layer2(i - 1, 1 - s)

            pe.wait_ge(scheduled, 1)
            turn(0, 0, 0)
            over_tiles(pe, body)
            layer2(N_TILES - 1, (N_TILES - 1) % 2)


def kernel(x, ctx_1024, g_xattn, g_ffn, L0_xattn_Wq, L0_xattn_Wkv, L0_xattn_Wc, L0_ffn_gate_w,
           L0_ffn_w1, L0_ffn_b1, L0_ffn_w2, L0_ffn_b2):
    import numpy as np
    import concourse.bacc as _bacc
    from concourse import mybir as _mybir
    from concourse.bass_utils import run_bass_kernel_spmd as _run

    arrays = {
        "x": np.asarray(x),
        "ctx_t": np.asarray(ctx_1024).transpose(0, 2, 1),
        "g": np.stack([np.asarray(g_xattn), np.asarray(g_ffn)], axis=1),
        "wq_t": np.asarray(L0_xattn_Wq).T,
        "wkv_t": np.asarray(L0_xattn_Wkv).T,
        "wc_t": np.asarray(L0_xattn_Wc).T,
        "gate_w": np.asarray(L0_ffn_gate_w),
        "w1": np.asarray(L0_ffn_w1),
        "b1_t": np.asarray(L0_ffn_b1).reshape(E, FC, P).transpose(2, 0, 1),
        "w2": np.asarray(L0_ffn_w2),
        "b2": np.asarray(L0_ffn_b2),
    }
    arrays = {name: np.ascontiguousarray(a) for name, a in arrays.items()}
    nc = _bacc.Bacc("TRN2", target_bir_lowering=False, num_devices=1)
    tensors = {name: nc.dram_tensor(name, a.shape, _mybir.dt.from_np(a.dtype), kind="ExternalInput").ap()
               for name, a in arrays.items()}
    out = nc.dram_tensor("out", (B, L, D), _mybir.dt.float32, kind="ExternalOutput").ap()
    program(nc, out=out, **tensors)
    nc.finalize()
    result = _run(nc, [arrays], core_ids=[0])
    return result.results[0]["out"]
```
